# Optimizing a Trainium2 kernel written in Bass

```python
import numpy as np
import jax
import jax.numpy as jnp

def _softmax(x, axis=-1):
    return jax.nn.softmax(x, axis=axis)

def _gelu(x):
    return jax.nn.gelu(x, approximate=True)

def _silu(x):
    return jax.nn.silu(x)

def _sigmoid(x):
    return jax.nn.sigmoid(x)

def _layernorm(x, axis=-1, eps=1e-05):
    m = jnp.mean(x, axis=axis, keepdims=True)
    v = jnp.var(x, axis=axis, keepdims=True)
    return (x - m) / jnp.sqrt(v + eps)

def _scatter_add(tgt, idx, src, axis=0):
    return tgt.at[idx].add(src)

def _segment_sum(src, seg, n):
    return jax.ops.segment_sum(src, seg, n)
kernel_name = 'mk_adj_preln_d1_adj_r2_10f0ae'

def setup_inputs(seed: int=0):
    np.random.seed(seed)
    _w = jnp.asarray

    def _rec_inputs():
        import jax
        import jax.numpy as jnp
        _gk = jax.random.key(seed)
        x = -0.0001538 + 1 * jax.random.normal(jax.random.fold_in(_gk, 1), (128, 128, 384), jnp.float32)
        _w = (1.0 + jnp.arange(128, dtype=jnp.float32)) ** (-0.5)
        _w = _w / _w.mean()
        _pij = jnp.clip(0.125 * _w[:, None] * _w[None, :], 0.0, 1.0)
        _a = jax.random.uniform(jax.random.fold_in(_gk, 2), (128, 128, 128)) < _pij
        _a = jnp.logical_or(_a, jnp.swapaxes(_a, -1, -2))
        _a = jnp.logical_or(_a, jnp.eye(128, dtype=bool))
        _af = _a.astype(jnp.float32)
        _af = _af * jax.random.uniform(jax.random.fold_in(_gk, 3), (128, 128, 128), jnp.float32, 0.05, 4.42607)
        adj = _af
        return (x, adj)
    x, adj = _rec_inputs()

    def _L0_gnn_setup():
        import jax, jax.numpy as jnp
        import numpy as np
        NUM_HEADS = 12
        HIDDEN = 384
        HEAD = HIDDEN // NUM_HEADS
        SCALE = HIDDEN ** (-0.5)
        key = jax.random.key(seed)
        ks = jax.random.split(key, 8)
        B, N = (16, 256)
        std = HIDDEN ** (-0.5)
        return {'x': jax.random.normal(ks[0], (B, N, HIDDEN), dtype=jnp.float32), 'encoding_bias': jax.random.normal(ks[1], (B, N, N), dtype=jnp.float32), 'Wq': jax.random.normal(ks[2], (HIDDEN, HIDDEN), dtype=jnp.float32) * std, 'Wk': jax.random.normal(ks[3], (HIDDEN, HIDDEN), dtype=jnp.float32) * std, 'Wv': jax.random.normal(ks[4], (HIDDEN, HIDDEN), dtype=jnp.float32) * std, 'bv': jax.random.normal(ks[5], (HIDDEN,), dtype=jnp.float32) * 0.01, 'Wo': jax.random.normal(ks[6], (HIDDEN, HIDDEN), dtype=jnp.float32) * std, 'bo': jax.random.normal(ks[7], (HIDDEN,), dtype=jnp.float32) * 0.01}
    _L0_gnn_all = _L0_gnn_setup()
    _L0_gnn_in = {k: v for k, v in _L0_gnn_all.items() if k in ('Wq', 'Wk', 'Wv', 'bv', 'Wo', 'bo')}
    del _L0_gnn_all
    return {'x': x, 'adj': adj, 'L0_gnn_Wq': _L0_gnn_in['Wq'], 'L0_gnn_Wk': _L0_gnn_in['Wk'], 'L0_gnn_Wv': _L0_gnn_in['Wv'], 'L0_gnn_bv': _L0_gnn_in['bv'], 'L0_gnn_Wo': _L0_gnn_in['Wo'], 'L0_gnn_bo': _L0_gnn_in['bo']}

def reference(x, adj, L0_gnn_Wq, L0_gnn_Wk, L0_gnn_Wv, L0_gnn_bv, L0_gnn_Wo, L0_gnn_bo):
    import jax
    import jax.numpy as jnp

    def _L0_gnn_ref(x, encoding_bias, Wq, Wk, Wv, bv, Wo, bo):
        import jax, jax.numpy as jnp
        import numpy as np
        NUM_HEADS = 12
        HIDDEN = 384
        HEAD = HIDDEN // NUM_HEADS
        SCALE = HIDDEN ** (-0.5)
        B, N, _ = x.shape
        q = (x @ Wq.T).reshape(B, N, NUM_HEADS, HEAD)
        k = (x @ Wk.T).reshape(B, N, NUM_HEADS, HEAD)
        v = (x @ Wv.T + bv).reshape(B, N, NUM_HEADS, HEAD)
        a = jnp.einsum('bnhd,bmhd->bhnm', q, k) * SCALE + encoding_bias[:, None, :, :]
        pad_mask = jnp.all(a == 0, axis=-1)
        a = jnp.where(pad_mask[..., None], -jnp.inf, a)
        a = jax.nn.softmax(a, axis=-1)
        a = jnp.nan_to_num(a)
        o = jnp.einsum('bhnm,bmhd->bnhd', a, v).reshape(B, N, HIDDEN)
        return o @ Wo.T + bo
    h = jnp.maximum(_layernorm(x, axis=-1), 0.0)
    x = x + _L0_gnn_ref(h, adj, L0_gnn_Wq, L0_gnn_Wk, L0_gnn_Wv, L0_gnn_bv, L0_gnn_Wo, L0_gnn_bo)
    return x

_drawn_inputs = setup_inputs


def setup_inputs(seed=0):
    import zlib

    import numpy as np

    out = dict(_drawn_inputs(seed))
    spreads = {}
    factors = {'L0_gnn_Wq': 3.928, 'L0_gnn_Wk': 3.898, 'L0_gnn_bv': 5.599, 'L0_gnn_bo': 6.18}
    for name, (base, spread) in spreads.items():
        noise = np.random.default_rng([zlib.crc32(name.encode()), seed]).standard_normal(out[name].shape)
        drawn = base * np.exp(spread * noise) if base else spread * noise
        out[name] = jnp.asarray(drawn.astype(out[name].dtype))
    for name, factor in factors.items():
        out[name] = (out[name] * factor).astype(out[name].dtype)
    return out
```

```python
from contextlib import ExitStack

import concourse.bass as bass
from concourse import mybir

F32 = mybir.dt.float32
F32R = mybir.dt.float32r
ALU = mybir.AluOpType
ACT = mybir.ActivationFunctionType
AX_X = mybir.AxisListType.X

HEADS = 12
GROUP = 2
SLOTS = 2 * GROUP
EPS = 1e-5
DMA = 16

TURNS = [(r, name) for r, names in enumerate([
    ["h_t0", "h_t1", "v0", "qk0", "av", "qk1", "qk2", "o"],
    ["v1", "qk3", "av", "qk4", "qk5", "o"],
]) for name in names]


def turn(step, name):
    return step // GROUP * len(TURNS) + TURNS.index((step % GROUP, name))


def group_of(step):
    return step - step % GROUP


def attention_layer(nc, x, adj, wq_t, wk_t, wv_t, wo_t, bv, bo, out):
    graphs, nodes, width = x.shape
    head = width // HEADS
    tiles = width // 128
    quads = 128 // head
    scale = float(width) ** -0.5
    bodies = graphs // SLOTS
    qk_tiles = 2 * tiles

    def count(body, graph, each=1, more=0):
        return body * (SLOTS * each) + (graph * each + more)

    def there(body, graph):
        return not isinstance(body, int) or 0 <= SLOTS * body + graph < graphs

    def wait(eng, semaphore, value):
        if not isinstance(value, int) or value > 0:
            eng.wait_ge(semaphore, value)

    def run(eng, step, ahead, peeled=1):
        last = bodies - 1 - -(-ahead // SLOTS)
        for s in range(-ahead, peeled * SLOTS):
            step(max(s // SLOTS, 0), s - max(s // SLOTS, 0) * SLOTS)
        with eng.Fori(peeled, last + 1) as body:
            for s in range(SLOTS):
                step(body, s)
        for s in range((last + 1) * SLOTS, graphs + 2):
            step(s // SLOTS, s % SLOTS)

    with ExitStack() as ctx:
        def sb(name, shape, dtype=F32):
            return ctx.enter_context(nc.sbuf_tensor(name, [128, *shape], dtype))

        def sem(name):
            return ctx.enter_context(nc.semaphore(name))

        identity = sb("identity", [128])
        minus_half = sb("minus_half", [1])
        minus_one = sb("minus_one", [1])
        eps_column = sb("eps_column", [1])
        bv_rows = sb("bv_rows", [width])
        bo_rows = sb("bo_rows", [width])
        w_names = ["q", "k", "v", "o"]
        w_full = {n: sb(f"w_{n}", [tiles, width]) for n in w_names}
        w_hi = {n: sb(f"w_{n}_hi", [tiles, width], F32R) for n in w_names}
        w_lo = {n: sb(f"w_{n}_lo", [tiles, width], F32R) for n in w_names}
        x_in = sb("x_in", [SLOTS, width])
        x_bo = sb("x_bo", [SLOTS, width])
        adj_in = sb("adj_in", [SLOTS, nodes])
        out_rows = sb("out_rows", [SLOTS, width])
        bn_parts = sb("bn_parts", [SLOTS, 6])
        mean_var = sb("mean_var", [SLOTS, 2])
        var_eps = sb("var_eps", [SLOTS, 1])
        minus_mean = sb("minus_mean", [SLOTS, 1])
        rstd = sb("rstd", [SLOTS, 1])
        h_rows = sb("h_rows", [GROUP, width])
        h_hi = sb("h_hi", [tiles, GROUP, nodes], F32R)
        h_lo = sb("h_lo", [tiles, GROUP, nodes], F32R)
        qk_t = sb("qk_t", [2, qk_tiles, GROUP, nodes])
        v_rows = sb("v_rows", [SLOTS, width])
        scores = sb("scores", [2, tiles, quads, nodes])
        minus_max = sb("minus_max", [2, HEADS])
        max_abs = sb("max_abs", [2, HEADS])
        probs = sb("probs", [2, HEADS, nodes])
        sums = sb("sums", [2, HEADS])
        inverse = sb("inverse", [2, HEADS])
        factor = sb("factor", [2, HEADS])
        attn = sb("attn", [2, HEADS, nodes])
        attn_t = sb("attn_t", [2, HEADS, nodes])
        o_hi = sb("o_hi", [2, tiles, nodes], F32R)
        o_lo = sb("o_lo", [2, tiles, nodes], F32R)

        ps_scores = [ctx.enter_context(nc.psum_tensor(f"ps_scores{j}", [128, 512], F32))
                     for j in range(quads)]
        ps_attn = [ctx.enter_context(nc.psum_tensor(f"ps_attn{n}", [128, 512], F32)) for n in range(2)]
        ps_turn = [ctx.enter_context(nc.psum_tensor(f"ps_turn{n}", [128, 512], F32)) for n in range(2)]

        s_weights = sem("s_weights")
        s_biases = sem("s_biases")
        s_x = [sem(f"s_x{s}") for s in range(SLOTS)]
        s_adj = [sem(f"s_adj{s}") for s in range(SLOTS)]
        s_stored = [sem(f"s_stored{s}") for s in range(SLOTS)]
        s_blank = sem("s_blank")
        s_constants = sem("s_constants")
        s_small = sem("s_small")
        s_h = sem("s_h")
        s_x_bo = sem("s_x_bo")
        s_attn = sem("s_attn")
        s_h_t = sem("s_h_t")
        s_qk = sem("s_qk")
        s_v = sem("s_v")
        s_scores = sem("s_scores")
        s_attn_t = sem("s_attn_t")
        s_av = sem("s_av")
        s_o = sem("s_o")
        s_h_hi = sem("s_h_hi")
        s_qk_out = sem("s_qk_out")
        s_exp = sem("s_exp")
        s_attn_t_out = sem("s_attn_t_out")
        s_o_hi = sem("s_o_hi")
        s_w_hi = sem("s_w_hi")
        s_w_lo = sem("s_w_lo")
        s_parts = sem("s_parts")
        s_stats = sem("s_stats")
        s_h_lo = sem("s_h_lo")
        s_v_out = sem("s_v_out")
        s_biased = sem("s_biased")
        s_max = sem("s_max")
        s_abs = sem("s_abs")
        s_inverse = sem("s_inverse")
        s_factor = sem("s_factor")
        s_o_lo = sem("s_o_lo")
        s_out = sem("s_out")

        block = ctx.enter_context(nc.Block())

        def rows(dram, body, graph):
            return dram[bass.ds(body * SLOTS + graph, 1), :, :].rearrange("g n d -> n (g d)")

        @block.sync
        def _(sp):
            def load_x(body, graph):
                wait(sp, s_x_bo, count(body, graph - SLOTS, 1, 1))
                slot = graph % SLOTS
                sp.dma_start(x_in[:, slot, :], rows(x, body, graph)).then_inc(s_x[slot], DMA)

            def load_adj(body, graph):
                wait(sp, s_biased, count(body, graph - SLOTS + 1, quads))
                slot = graph % SLOTS
                sp.dma_start(adj_in[:, slot, :], rows(adj, body, graph)).then_inc(s_adj[slot], DMA)

            def step(body, s):
                if there(body, s + 3):
                    load_adj(body, s + 3)
                if there(body, s - 2):
                    slot = (s - 2) % SLOTS
                    sp.wait_ge(s_out, count(body, s - 2, 1, 1))
                    sp.dma_start(rows(out, body, s - 2), out_rows[:, slot, :]).then_inc(s_stored[slot], DMA)
                if there(body, s + GROUP) and there(body, s + SLOTS + GROUP):
                    load_x(body, s + SLOTS + GROUP)

            for g in range(SLOTS):
                load_x(0, g)
            for n, w in zip(w_names, [wq_t, wk_t, wv_t, wo_t]):
                sp.dma_start(w_full[n][:], w.rearrange("(t p) n -> p t n", p=128)).then_inc(s_weights, DMA)
            sp.dma_start(bo_rows[:], bo.partition_broadcast(128)).then_inc(s_biases, DMA)
            sp.dma_start(bv_rows[:], bv.partition_broadcast(128)).then_inc(s_biases, DMA)
            run(sp, step, SLOTS + GROUP)
            for s in range(SLOTS):
                sp.wait_ge(s_stored[s], DMA * bodies)

        @block.gpsimd
        def _(pool):
            def scale_of_h(body, graph):
                slot = graph % SLOTS
                pool.wait_ge(s_stats, count(body, graph, 1, 1))
                nc.gpsimd.tensor_tensor(var_eps[:, slot, :], mean_var[:, slot, 1:2], eps_column[:],
                                        ALU.add).then_inc(s_small, 1)
                nc.gpsimd.tensor_tensor(minus_mean[:, slot, :], mean_var[:, slot, 0:1], minus_one[:],
                                        ALU.mult).then_inc(s_small, 1)
                pool.wait_ge(s_small, count(body, graph, 3, 2))
                nc.gpsimd.tensor_tensor(rstd[:, slot, :], var_eps[:, slot, :], minus_half[:],
                                        ALU.pow).then_inc(s_small, 1)

            def wait_for_h(body, graph):
                pool.wait_ge(s_small, count(body, graph, 3, 3))
                wait(pool, s_h_t, count(body, graph - GROUP, 1, 1))

            def make_h(body, graph):
                slot = graph % SLOTS
                nc.gpsimd.tensor_scalar(h_rows[:, graph % GROUP, :], x_in[:, slot, :],
                                        minus_mean[:, slot, :], rstd[:, slot, :],
                                        ALU.add, ALU.mult).then_inc(s_h, 1)

            def add_bo(body, graph):
                slot = graph % SLOTS
                wait(pool, s_out, count(body, graph - SLOTS, 1, 1))
                nc.gpsimd.tensor_tensor(x_bo[:, slot, :], x_in[:, slot, :], bo_rows[:],
                                        ALU.add).then_inc(s_x_bo, 1)

            def normalise(body, graph):
                pool.wait_ge(s_factor, count(body, graph, 1, 1))
                wait(pool, s_attn_t, count(body, graph - 1, tiles))
                b = graph % 2
                for t in range(tiles):
                    of = slice(t * quads, (t + 1) * quads)
                    nc.gpsimd.tensor_tensor(
                        attn[:, b, of, :], probs[:, b, of, :],
                        factor[:, b, of].unsqueeze(2).to_broadcast([128, quads, nodes]),
                        ALU.mult).then_inc(s_attn, 1)

            def step(body, s):
                if there(body, s - 1):
                    normalise(body, s - 1)
                if there(body, s + SLOTS):
                    scale_of_h(body, s + SLOTS)
                    wait_for_h(body, s + SLOTS)
                if there(body, s + GROUP):
                    add_bo(body, s + GROUP)
                if there(body, s + SLOTS):
                    make_h(body, s + SLOTS)

            nc.gpsimd.memset(identity[:], 0.0).then_inc(s_blank, 1)
            nc.gpsimd.memset(minus_half[:], -0.5).then_inc(s_constants, 1)
            nc.gpsimd.memset(minus_one[:], -1.0).then_inc(s_constants, 1)
            nc.gpsimd.memset(eps_column[:], EPS).then_inc(s_constants, 1)
            pool.wait_ge(s_blank, 1)
            nc.gpsimd.affine_select(out=identity[:], in_=identity[:], compare_op=ALU.not_equal,
                                    fill=1.0, base=0, pattern=[[-1, 128]],
                                    channel_multiplier=1).then_inc(s_constants, 1)
            pool.wait_ge(s_constants, 4)
            pool.wait_ge(s_biases, 2 * DMA)
            run(pool, step, SLOTS)

        @block.tensor
        def _(pe):
            def bank(body, s, name):
                before = turn(s, name) - 2
                while before >= turn(-GROUP, "h_t0"):
                    of, (r, n) = before // len(TURNS) * GROUP, TURNS[before % len(TURNS)]
                    if n in ("av", "o") and there(body, of + r - 1):
                        pe.wait_ge(s_o_lo if n == "av" else s_out, count(body, of + r - 1, 1, 1))
                        break
                    if n.startswith("qk") and there(body, of + GROUP):
                        pe.wait_ge(s_qk_out, count(body, of + GROUP, qk_tiles // GROUP, int(n[-1]) + 1))
                        break
                    if n[0] in "hv" and there(body, of + GROUP):
                        pe.wait_ge(s_h_lo if n[0] == "h" else s_v_out,
                                   count(body, of + GROUP + int(n[-1]), 1, 1))
                        break
                    before -= 2
                return ps_turn[turn(s, name) % 2]

            def transpose_h(body, s, first, g):
                ps = bank(body, s, f"h_t{g}")
                pe.wait_ge(s_h, count(body, first + g, 1, 1))
                for t in range(tiles):
                    last = nc.tensor.transpose(ps[:, t * nodes:(t + 1) * nodes],
                                               h_rows[:, g, t * 128:(t + 1) * 128], identity[:])
                last.then_inc(s_h_t, 1)

            def split_product(ps, left, right):
                parts = [(0, 0), (0, 1), (1, 0)]
                for t in range(tiles):
                    for n, (a, b) in enumerate(parts):
                        last = nc.tensor.matmul(ps, left(a, t), right(b, t), start=(t == 0 and n == 0),
                                                stop=(t == tiles - 1 and n == len(parts) - 1))
                return last

            def project_qk(body, s, first, tile):
                ps = bank(body, s, f"qk{tile}")
                pe.wait_ge(s_h_lo, count(body, first + GROUP))
                name, c = w_names[tile // tiles], tile % tiles
                split_product(ps[:, 0:GROUP * nodes],
                              lambda a, t: (w_hi, w_lo)[a][name][:, t, c * 128:(c + 1) * 128],
                              lambda b, t: (h_hi, h_lo)[b][:, t, :, :]).then_inc(s_qk, 1)

            def project_v(body, s, first, g):
                ps = bank(body, s, f"v{g}")
                pe.wait_ge(s_h_lo, count(body, first + g, 1, 1))
                split_product(ps[:, 0:width],
                              lambda a, t: (h_hi, h_lo)[a][:, t, g, :],
                              lambda b, t: (w_hi, w_lo)[b]["v"][:, t, :]).then_inc(s_v, 1)

            def make_scores(body, graph):
                first = group_of(graph)
                pair = graph // GROUP % 2
                pe.wait_ge(s_qk_out, count(body, first + GROUP, qk_tiles // GROUP))
                for t in range(tiles):
                    for j in range(quads):
                        if t == 0:
                            wait(pe, s_biased, count(body, graph - 1, quads, j + 1))
                        of = slice(j * head, (j + 1) * head)
                        last = nc.tensor.matmul(ps_scores[j][:, t * nodes:(t + 1) * nodes],
                                                qk_t[of, pair, t, graph % GROUP, :],
                                                qk_t[of, pair, tiles + t, graph % GROUP, :],
                                                start=True, stop=True)
                        if t == tiles - 1:
                            last.then_inc(s_scores, 1)

            def transpose_attn(body, graph, t):
                n = (graph % SLOTS) * tiles + t
                pe.wait_ge(s_attn, count(body, graph, tiles, t + 1))
                wait(pe, s_attn_t_out, count(body, graph, tiles, t - 1))
                for j in range(quads):
                    last = nc.tensor.transpose(ps_attn[n % 2][:, j * nodes:(j + 1) * nodes],
                                               attn[:, graph % 2, t * quads + j, :], identity[:])
                last.then_inc(s_attn_t, 1)

            def attend(body, s, graph):
                ps = bank(body, s, "av")
                pe.wait_ge(s_attn_t_out, count(body, graph + 1, tiles))
                pe.wait_ge(s_v_out, count(body, graph, 1, 1))
                for t in range(tiles):
                    for j in range(quads):
                        c = (t * quads + j) * head
                        last = nc.tensor.matmul(ps[j * head:(j + 1) * head, t * nodes:(t + 1) * nodes],
                                                v_rows[:, graph % SLOTS, c:c + head],
                                                attn_t[:, graph % 2, t * quads + j, :],
                                                start=True, stop=True)
                last.then_inc(s_av, 1)

            def project_out(body, s, graph):
                ps = bank(body, s, "o")
                pe.wait_ge(s_o_lo, count(body, graph, 1, 1))
                split_product(ps[:, 0:width],
                              lambda a, t: (o_hi, o_lo)[a][:, graph % 2, t, :],
                              lambda b, t: (w_hi, w_lo)[b]["o"][:, t, :]).then_inc(s_o, 1)

            def step(body, s):
                now = group_of(s)
                ahead = there(body, now + GROUP)
                k = s % GROUP
                if k == 0 and ahead:
                    for g in range(GROUP):
                        transpose_h(body, s, now + GROUP, g)
                if isinstance(body, int) and SLOTS * body + s == -GROUP:
                    pe.wait_ge(s_w_lo, len(w_names))
                if there(body, s):
                    make_scores(body, s)
                if there(body, s - 1):
                    transpose_attn(body, s - 1, 0)
                    transpose_attn(body, s - 1, 1)
                if ahead:
                    project_v(body, s, now + GROUP, k)
                if there(body, s - 1):
                    transpose_attn(body, s - 1, 2)
                if ahead:
                    project_qk(body, s, now + GROUP, 3 * k)
                if there(body, s - 1):
                    attend(body, s, s - 1)
                if ahead:
                    project_qk(body, s, now + GROUP, 3 * k + 1)
                    project_qk(body, s, now + GROUP, 3 * k + 2)
                if there(body, s - 1):
                    project_out(body, s, s - 1)

            pe.wait_ge(s_constants, 4)
            run(pe, step, GROUP)

        @block.scalar
        def _(act):
            def round_h(body, first, g):
                wait(act, s_qk, count(body, first, qk_tiles // GROUP))
                wait(act, s_v, count(body, first))
                act.wait_ge(s_h_t, count(body, first + g, 1, 1))
                nc.scalar.activation(h_hi[:, :, g, :],
                                     ps_turn[turn(first - GROUP, f"h_t{g}") % 2][:, 0:width].rearrange(
                                         "p (t n) -> p t n", t=tiles), ACT.Relu).then_inc(s_h_hi, 1)

            def copy_qk(body, first, tile):
                pair = first // GROUP % 2
                act.wait_ge(s_qk, count(body, first, qk_tiles // GROUP, tile + 1))
                wait(act, s_scores, count(body, first - GROUP, quads))
                nc.scalar.activation(qk_t[:, pair, tile, :, :],
                                     ps_turn[turn(first - GROUP + tile // 3, f"qk{tile}") % 2][
                                         :, 0:GROUP * nodes].rearrange("p (g n) -> p g n", g=GROUP),
                                     ACT.Copy).then_inc(s_qk_out, 1)

            def copy_attn_t(body, graph, t):
                n = (graph % SLOTS) * tiles + t
                act.wait_ge(s_attn_t, count(body, graph, tiles, t + 1))
                wait(act, s_av, count(body, graph - 1))
                nc.scalar.activation(attn_t[:, graph % 2, t * quads:(t + 1) * quads, :],
                                     ps_attn[n % 2][:].rearrange("p (j n) -> p j n", j=quads),
                                     ACT.Copy).then_inc(s_attn_t_out, 1)

            def exponentials(body, graph, t):
                b = graph % 2
                if t == 0:
                    act.wait_ge(s_max, count(body, graph, 1, 1))
                    wait(act, s_attn, count(body, graph - 1, tiles))
                for h in range(t * quads, (t + 1) * quads):
                    last = nc.scalar.activation(probs[:, b, h, :], scores[:, b, h // quads, h % quads, :],
                                                ACT.Exp, bias=minus_max[:, b, h:h + 1],
                                                accum_out=sums[:, b, h:h + 1])
                if t == tiles - 1:
                    last.then_inc(s_exp, 1)

            def round_o(body, graph):
                act.wait_ge(s_av, count(body, graph, 1, 1))
                wait(act, s_o, count(body, graph - 1))
                nc.scalar.activation(o_hi[:, graph % 2, :, :],
                                     ps_turn[turn(graph + 1, "av") % 2][:, 0:width].rearrange(
                                         "p (t n) -> p t n", t=tiles), ACT.Copy).then_inc(s_o_hi, 1)

            def step(body, s):
                now = group_of(s)
                ahead = there(body, now + GROUP)
                k = s % GROUP
                if k == 0 and ahead:
                    for g in range(GROUP):
                        round_h(body, now + GROUP, g)
                if there(body, s - 1):
                    for t in range(tiles):
                        copy_attn_t(body, s - 1, t)
                if ahead:
                    copy_qk(body, now + GROUP, 3 * k)
                if there(body, s):
                    exponentials(body, s, 0)
                if there(body, s - 1):
                    round_o(body, s - 1)
                if ahead:
                    copy_qk(body, now + GROUP, 3 * k + 1)
                if there(body, s):
                    exponentials(body, s, 1)
                if ahead:
                    copy_qk(body, now + GROUP, 3 * k + 2)
                if there(body, s):
                    exponentials(body, s, 2)

            run(act, step, GROUP)

        @block.vector
        def _(dve):
            def split_weights():
                dve.wait_ge(s_weights, DMA * len(w_names))
                for n in w_names:
                    nc.vector.tensor_copy(w_hi[n][:], w_full[n][:]).then_inc(s_w_hi, 1)
                for k, n in enumerate(w_names):
                    dve.wait_ge(s_w_hi, k + 1)
                    nc.vector.tensor_tensor(w_lo[n][:], w_full[n][:], w_hi[n][:].bitcast(F32),
                                            ALU.subtract).then_inc(s_w_lo, 1)

            def statistics(body, graph):
                slot = graph % SLOTS
                dve.wait_ge(s_x[slot], DMA * (body + (graph // SLOTS + 1)))
                nc.vector.bn_stats(bn_parts[:, slot, :], x_in[:, slot, :]).then_inc(s_parts, 1)

            def wait_for_mean(body, graph):
                dve.wait_ge(s_parts, count(body, graph, 1, 1))
                wait(dve, s_h, count(body, graph - SLOTS, 1, 1))

            def mean(body, graph):
                slot = graph % SLOTS
                nc.vector.bn_aggr(mean_var[:, slot, :], bn_parts[:, slot, :]).then_inc(s_stats, 1)

            def rest_of_h(body, first, g):
                dve.wait_ge(s_h_hi, count(body, first + g, 1, 1))
                nc.vector.scalar_tensor_tensor(
                    out=h_lo[:, :, g, :],
                    in0=ps_turn[turn(first - GROUP, f"h_t{g}") % 2][:, 0:width].rearrange(
                        "p (t n) -> p t n", t=tiles),
                    scalar=0.0, in1=h_hi[:, :, g, :].bitcast(F32),
                    op0=ALU.max, op1=ALU.subtract).then_inc(s_h_lo, 1)

            def bias_v(body, first, g):
                dve.wait_ge(s_v, count(body, first + g, 1, 1))
                wait(dve, s_av, count(body, first + g - SLOTS, 1, 1))
                nc.vector.tensor_tensor(v_rows[:, (first + g) % SLOTS, :],
                                        ps_turn[turn(first - GROUP + g, f"v{g}") % 2][:, 0:width],
                                        bv_rows[:], ALU.add).then_inc(s_v_out, 1)

            def bias_scores(body, graph):
                slot = graph % SLOTS
                dve.wait_ge(s_adj[slot], DMA * (body + (graph // SLOTS + 1)))
                wait(dve, s_exp, count(body, graph - 1))
                for j in range(quads):
                    dve.wait_ge(s_scores, count(body, graph, quads, j + 1))
                    nc.vector.scalar_tensor_tensor(
                        out=scores[:, graph % 2, :, j, :],
                        in0=ps_scores[j][:, 0:tiles * nodes].rearrange("p (t m) -> p t m", t=tiles),
                        scalar=scale,
                        in1=adj_in[:, slot:slot + 1, :].to_broadcast([128, tiles, nodes]),
                        op0=ALU.mult, op1=ALU.add).then_inc(s_biased, 1)

            def maxima(body, graph):
                dve.wait_ge(s_biased, count(body, graph + 1, quads))
                of = scores[:, graph % 2, :, :, :].rearrange("p t j m -> p (t j) m")
                nc.vector.tensor_reduce(minus_max[:, graph % 2, :], of, AX_X, ALU.max,
                                        negate=True).then_inc(s_max, 1)
                nc.vector.tensor_reduce(max_abs[:, graph % 2, :], of, AX_X, ALU.max,
                                        apply_absolute_value=True).then_inc(s_abs, 1)

            def factors(body, graph):
                b = graph % 2
                dve.wait_ge(s_exp, count(body, graph, 1, 1))
                nc.vector.reciprocal(inverse[:, b, :], sums[:, b, :]).then_inc(s_inverse, 1)
                dve.wait_ge(s_inverse, count(body, graph, 1, 1))
                dve.wait_ge(s_abs, count(body, graph, 1, 1))
                wait(dve, s_attn, count(body, graph - 1, tiles))
                nc.vector.scalar_tensor_tensor(out=factor[:, b, :], in0=max_abs[:, b, :], scalar=0.0,
                                               in1=inverse[:, b, :], op0=ALU.is_gt,
                                               op1=ALU.mult).then_inc(s_factor, 1)

            def rest_of_o(body, graph):
                dve.wait_ge(s_o_hi, count(body, graph, 1, 1))
                nc.vector.tensor_tensor(
                    o_lo[:, graph % 2, :, :],
                    ps_turn[turn(graph + 1, "av") % 2][:, 0:width].rearrange("p (t n) -> p t n", t=tiles),
                    o_hi[:, graph % 2, :, :].bitcast(F32), ALU.subtract).then_inc(s_o_lo, 1)

            def make_out(body, graph):
                slot = graph % SLOTS
                dve.wait_ge(s_o, count(body, graph, 1, 1))
                dve.wait_ge(s_x_bo, count(body, graph, 1, 1))
                wait(dve, s_stored[slot], DMA * (body + graph // SLOTS))
                nc.vector.tensor_tensor(out_rows[:, slot, :],
                                        ps_turn[turn(graph + 1, "o") % 2][:, 0:width],
                                        x_bo[:, slot, :], ALU.add).then_inc(s_out, 1)

            def step(body, s):
                now = group_of(s)
                ahead = there(body, now + GROUP)
                k = s % GROUP
                if there(body, s - 2):
                    make_out(body, s - 2)
                if there(body, s - 1):
                    factors(body, s - 1)
                if k == 0 and ahead:
                    for g in range(GROUP):
                        rest_of_h(body, now + GROUP, g)
                if there(body, s):
                    bias_scores(body, s)
                if ahead:
                    bias_v(body, now + GROUP, k)
                if there(body, s):
                    maxima(body, s)
                if there(body, s + SLOTS):
                    statistics(body, s + SLOTS)
                    wait_for_mean(body, s + SLOTS)
                if there(body, s - 1):
                    rest_of_o(body, s - 1)
                if there(body, s + SLOTS):
                    mean(body, s + SLOTS)
                if isinstance(body, int) and SLOTS * body + s == -GROUP - 1:
                    split_weights()
                    dve.wait_ge(s_biases, 2 * DMA)

            run(dve, step, SLOTS, peeled=2)


_INS = ["x", "adj", "L0_gnn_Wq", "L0_gnn_Wk", "L0_gnn_Wv", "L0_gnn_Wo", "L0_gnn_bv", "L0_gnn_bo"]


def kernel(**inputs):
    import numpy as np
    import concourse.bacc as bacc
    from concourse.bass_utils import run_bass_kernel_spmd

    nc = bacc.Bacc("TRN2", target_bir_lowering=False, num_devices=1)
    arrays, args = {}, []
    for name in _INS:
        a = np.asarray(inputs[name])
        if "_W" in name:
            a = a.T
        a = np.ascontiguousarray(a)
        arrays[f"in_{name}"] = a
        args.append(nc.dram_tensor(f"in_{name}", a.shape, mybir.dt.from_np(a.dtype), kind="ExternalInput").ap())
    shape = inputs["x"].shape
    args.append(nc.dram_tensor("out_rows_dram", shape, F32, kind="ExternalOutput").ap())
    attention_layer(nc, *args)
    r = run_bass_kernel_spmd(nc, [arrays], core_ids=[0])
    return r.results[0]["out_rows_dram"]
```

```python
from contextlib import ExitStack

import concourse.bass as bass
from concourse import mybir

F32 = mybir.dt.float32
F32R = mybir.dt.float32r
ALU = mybir.AluOpType
ACT = mybir.ActivationFunctionType
AX_X = mybir.AxisListType.X

HEADS = 12
GROUP = 2
SLOTS = 2 * GROUP
EPS = 1e-5
DMA = 16

TURNS = [(r, name) for r, names in enumerate([
    ["h_t0", "h_t1", "o", "qk0", "qk1", "qk2", "av", "v0"],
    ["o", "qk3", "qk4", "qk5", "av", "v1"],
]) for name in names]


def turn(step, name):
    return step // GROUP * len(TURNS) + TURNS.index((step % GROUP, name))


def group_of(step):
    return step - step % GROUP


def attention_layer(nc, x, adj, wq_t, wk_t, wv_t, wo_t, bv, bo, out):
    graphs, nodes, width = x.shape
    head = width // HEADS
    tiles = width // 128
    quads = 128 // head
    scale = float(width) ** -0.5
    bodies = graphs // SLOTS
    qk_tiles = 2 * tiles

    def count(body, graph, each=1, more=0):
        return body * (SLOTS * each) + (graph * each + more)

    def there(body, graph):
        return not isinstance(body, int) or 0 <= SLOTS * body + graph < graphs

    def wait(eng, semaphore, value):
        if not isinstance(value, int) or value > 0:
            eng.wait_ge(semaphore, value)

    def run(eng, step, ahead, peeled=1):
        last = bodies - 1 - -(-ahead // SLOTS)
        for s in range(-ahead, peeled * SLOTS):
            step(max(s // SLOTS, 0), s - max(s // SLOTS, 0) * SLOTS)
        with eng.Fori(peeled, last + 1) as body:
            for s in range(SLOTS):
                step(body, s)
        for s in range((last + 1) * SLOTS, graphs + 3):
            step(s // SLOTS, s % SLOTS)

    with ExitStack() as ctx:
        def sb(name, shape, dtype=F32):
            return ctx.enter_context(nc.sbuf_tensor(name, [128, *shape], dtype))

        def sem(name):
            return ctx.enter_context(nc.semaphore(name))

        identity = sb("identity", [128])
        minus_half = sb("minus_half", [1])
        minus_one = sb("minus_one", [1])
        eps_column = sb("eps_column", [1])
        bv_rows = sb("bv_rows", [width])
        bo_rows = sb("bo_rows", [width])
        w_names = ["q", "k", "v", "o"]
        w_full = {n: sb(f"w_{n}", [tiles, width]) for n in w_names}
        w_hi = {n: sb(f"w_{n}_hi", [tiles, width], F32R) for n in w_names}
        w_lo = {n: sb(f"w_{n}_lo", [tiles, width], F32R) for n in w_names}
        x_in = sb("x_in", [SLOTS, width])
        x_bo = sb("x_bo", [SLOTS, width])
        adj_in = sb("adj_in", [SLOTS, nodes])
        out_rows = sb("out_rows", [SLOTS, width])
        bn_parts = sb("bn_parts", [SLOTS, 6])
        mean_var = sb("mean_var", [SLOTS, 2])
        var_eps = sb("var_eps", [SLOTS, 1])
        minus_mean = sb("minus_mean", [SLOTS, 1])
        rstd = sb("rstd", [SLOTS, 1])
        h_rows = sb("h_rows", [GROUP, width])
        h_hi = sb("h_hi", [tiles, GROUP, nodes], F32R)
        h_lo = sb("h_lo", [tiles, GROUP, nodes], F32R)
        qk_t = sb("qk_t", [2, qk_tiles, GROUP, nodes])
        v_rows = sb("v_rows", [SLOTS, width])
        scores = sb("scores", [2, tiles, quads, nodes])
        minus_max = sb("minus_max", [2, HEADS])
        max_abs = sb("max_abs", [2, HEADS])
        probs = sb("probs", [2, HEADS, nodes])
        sums = sb("sums", [2, HEADS])
        inverse = sb("inverse", [2, HEADS])
        factor = sb("factor", [2, HEADS])
        attn = sb("attn", [2, HEADS, nodes])
        attn_t = sb("attn_t", [2, HEADS, nodes])
        o_hi = sb("o_hi", [2, tiles, nodes], F32R)
        o_lo = sb("o_lo", [2, tiles, nodes], F32R)

        ps_scores = [ctx.enter_context(nc.psum_tensor(f"ps_scores{j}", [128, 512], F32))
                     for j in range(quads)]
        ps_attn = [ctx.enter_context(nc.psum_tensor(f"ps_attn{n}", [128, 512], F32)) for n in range(2)]
        ps_turn = [ctx.enter_context(nc.psum_tensor(f"ps_turn{n}", [128, 512], F32)) for n in range(2)]

        s_weights = {n: sem(f"s_weights_{n}") for n in w_names}
        s_bo = sem("s_bo")
        s_bv = sem("s_bv")
        s_x = [sem(f"s_x{s}") for s in range(SLOTS)]
        s_adj = [sem(f"s_adj{s}") for s in range(SLOTS)]
        s_stored = [sem(f"s_stored{s}") for s in range(SLOTS)]
        s_blank = sem("s_blank")
        s_constants = sem("s_constants")
        s_small = sem("s_small")
        s_h = sem("s_h")
        s_x_bo = sem("s_x_bo")
        s_attn = sem("s_attn")
        s_h_t = sem("s_h_t")
        s_qk = sem("s_qk")
        s_v = sem("s_v")
        s_scores = sem("s_scores")
        s_attn_t = sem("s_attn_t")
        s_av = sem("s_av")
        s_o = sem("s_o")
        s_w_hi = sem("s_w_hi")
        s_h_hi = sem("s_h_hi")
        s_qk_out = sem("s_qk_out")
        s_exp = sem("s_exp")
        s_attn_t_out = sem("s_attn_t_out")
        s_o_hi = sem("s_o_hi")
        s_w_lo = sem("s_w_lo")
        s_parts = sem("s_parts")
        s_stats = sem("s_stats")
        s_h_lo = sem("s_h_lo")
        s_v_out = sem("s_v_out")
        s_biased = sem("s_biased")
        s_max = sem("s_max")
        s_abs = sem("s_abs")
        s_inverse = sem("s_inverse")
        s_factor = sem("s_factor")
        s_o_lo = sem("s_o_lo")
        s_out = sem("s_out")

        block = ctx.enter_context(nc.Block())

        def rows(dram, body, graph):
            return dram[bass.ds(body * SLOTS + graph, 1), :, :].rearrange("g n d -> n (g d)")

        @block.sync
        def _(sp):
            def load_x(body, graph):
                wait(sp, s_x_bo, count(body, graph - SLOTS, 1, 1))
                slot = graph % SLOTS
                sp.dma_start(x_in[:, slot, :], rows(x, body, graph)).then_inc(s_x[slot], DMA)

            def load_adj(body, graph):
                wait(sp, s_biased, count(body, graph - SLOTS + 1, quads))
                slot = graph % SLOTS
                sp.dma_start(adj_in[:, slot, :], rows(adj, body, graph)).then_inc(s_adj[slot], DMA)

            def step(body, s):
                if there(body, s + 3):
                    load_adj(body, s + 3)
                if there(body, s - 3):
                    slot = (s - 3) % SLOTS
                    sp.wait_ge(s_out, count(body, s - 3, 1, 1))
                    sp.dma_start(rows(out, body, s - 3), out_rows[:, slot, :]).then_inc(s_stored[slot], DMA)
                if there(body, s + 1) and there(body, s + 1 + SLOTS):
                    load_x(body, s + 1 + SLOTS)

            def load_weights(n, w):
                sp.dma_start(w_full[n][:], w.rearrange("(t p) n -> p t n", p=128)).then_inc(s_weights[n], DMA)

            for g in range(GROUP):
                load_x(0, g)
            load_weights("q", wq_t)
            load_weights("k", wk_t)
            load_weights("v", wv_t)
            sp.dma_start(bv_rows[:], bv.partition_broadcast(128)).then_inc(s_bv, DMA)
            sp.dma_start(bo_rows[:], bo.partition_broadcast(128)).then_inc(s_bo, DMA)
            for g in range(GROUP, SLOTS):
                load_x(0, g)
            load_weights("o", wo_t)
            run(sp, step, SLOTS + 1)
            for s in range(SLOTS):
                sp.wait_ge(s_stored[s], DMA * bodies)

        @block.gpsimd
        def _(pool):
            def scale_of_h(body, graph):
                slot = graph % SLOTS
                pool.wait_ge(s_stats, count(body, graph, 1, 1))
                nc.gpsimd.tensor_tensor(var_eps[:, slot, :], mean_var[:, slot, 1:2], eps_column[:],
                                        ALU.add).then_inc(s_small, 1)
                nc.gpsimd.tensor_tensor(minus_mean[:, slot, :], mean_var[:, slot, 0:1], minus_one[:],
                                        ALU.mult).then_inc(s_small, 1)
                pool.wait_ge(s_small, count(body, graph, 3, 2))
                nc.gpsimd.tensor_tensor(rstd[:, slot, :], var_eps[:, slot, :], minus_half[:],
                                        ALU.pow).then_inc(s_small, 1)

            def wait_for_h(body, graph):
                pool.wait_ge(s_small, count(body, graph, 3, 3))
                wait(pool, s_h_t, count(body, graph - GROUP, 1, 1))

            def make_h(body, graph):
                slot = graph % SLOTS
                nc.gpsimd.tensor_scalar(h_rows[:, graph % GROUP, :], x_in[:, slot, :],
                                        minus_mean[:, slot, :], rstd[:, slot, :],
                                        ALU.add, ALU.mult).then_inc(s_h, 1)

            def add_bo(body, graph):
                slot = graph % SLOTS
                if isinstance(body, int) and body == graph == 0:
                    pool.wait_ge(s_bo, DMA)
                wait(pool, s_out, count(body, graph - SLOTS, 1, 1))
                nc.gpsimd.tensor_tensor(x_bo[:, slot, :], x_in[:, slot, :], bo_rows[:],
                                        ALU.add).then_inc(s_x_bo, 1)

            def normalise(body, graph):
                pool.wait_ge(s_factor, count(body, graph, 1, 1))
                wait(pool, s_attn_t, count(body, graph - 1, tiles))
                b = graph % 2
                for t in range(tiles):
                    of = slice(t * quads, (t + 1) * quads)
                    nc.gpsimd.tensor_tensor(
                        attn[:, b, of, :], probs[:, b, of, :],
                        factor[:, b, of].unsqueeze(2).to_broadcast([128, quads, nodes]),
                        ALU.mult).then_inc(s_attn, 1)

            def step(body, s):
                if there(body, s - 1):
                    normalise(body, s - 1)
                if there(body, s + SLOTS):
                    scale_of_h(body, s + SLOTS)
                    wait_for_h(body, s + SLOTS)
                if there(body, s + 1):
                    add_bo(body, s + 1)
                if there(body, s + SLOTS):
                    make_h(body, s + SLOTS)

            nc.gpsimd.memset(identity[:], 0.0).then_inc(s_blank, 1)
            nc.gpsimd.memset(minus_half[:], -0.5).then_inc(s_constants, 1)
            nc.gpsimd.memset(minus_one[:], -1.0).then_inc(s_constants, 1)
            nc.gpsimd.memset(eps_column[:], EPS).then_inc(s_constants, 1)
            pool.wait_ge(s_blank, 1)
            nc.gpsimd.affine_select(out=identity[:], in_=identity[:], compare_op=ALU.not_equal,
                                    fill=1.0, base=0, pattern=[[-1, 128]],
                                    channel_multiplier=1).then_inc(s_constants, 1)
            pool.wait_ge(s_constants, 4)
            run(pool, step, SLOTS)

        @block.tensor
        def _(pe):
            def bank(body, s, name):
                before = turn(s, name) - 2
                while before >= turn(-GROUP, "h_t0"):
                    of, (r, n) = before // len(TURNS) * GROUP, TURNS[before % len(TURNS)]
                    if n == "av" and there(body, of + r - 2):
                        pe.wait_ge(s_o_lo, count(body, of + r - 2, 1, 1))
                        break
                    if n == "o" and there(body, of + r - 3):
                        pe.wait_ge(s_out, count(body, of + r - 3, 1, 1))
                        break
                    if n.startswith("qk") and there(body, of + GROUP):
                        pe.wait_ge(s_qk_out, count(body, of + GROUP, qk_tiles // GROUP, int(n[-1]) + 1))
                        break
                    if n[0] in "hv" and there(body, of + GROUP):
                        pe.wait_ge(s_h_lo if n[0] == "h" else s_v_out,
                                   count(body, of + GROUP + int(n[-1]), 1, 1))
                        break
                    before -= 2
                return ps_turn[turn(s, name) % 2]

            def transpose_h(body, s, first, g):
                ps = bank(body, s, f"h_t{g}")
                pe.wait_ge(s_h, count(body, first + g, 1, 1))
                for t in range(tiles):
                    last = nc.tensor.transpose(ps[:, t * nodes:(t + 1) * nodes],
                                               h_rows[:, g, t * 128:(t + 1) * 128], identity[:])
                last.then_inc(s_h_t, 1)

            def split_product(ps, left, right):
                parts = [(0, 0), (0, 1), (1, 0)]
                for t in range(tiles):
                    for n, (a, b) in enumerate(parts):
                        last = nc.tensor.matmul(ps, left(a, t), right(b, t), start=(t == 0 and n == 0),
                                                stop=(t == tiles - 1 and n == len(parts) - 1))
                return last

            def wait_for_weight(body, graph, n):
                if isinstance(body, int) and body == graph == 0:
                    pe.wait_ge(s_w_lo, n + 1)

            def project_qk(body, s, first, tile):
                ps = bank(body, s, f"qk{tile}")
                pe.wait_ge(s_h_lo, count(body, first + GROUP))
                wait_for_weight(body, first, tile // tiles)
                name, c = w_names[tile // tiles], tile % tiles
                split_product(ps[:, 0:GROUP * nodes],
                              lambda a, t: (w_hi, w_lo)[a][name][:, t, c * 128:(c + 1) * 128],
                              lambda b, t: (h_hi, h_lo)[b][:, t, :, :]).then_inc(s_qk, 1)

            def project_v(body, s, first, g):
                ps = bank(body, s, f"v{g}")
                pe.wait_ge(s_h_lo, count(body, first + g, 1, 1))
                wait_for_weight(body, first, w_names.index("v"))
                split_product(ps[:, 0:width],
                              lambda a, t: (h_hi, h_lo)[a][:, t, g, :],
                              lambda b, t: (w_hi, w_lo)[b]["v"][:, t, :]).then_inc(s_v, 1)

            def make_scores(body, graph):
                first = group_of(graph)
                pair = graph // GROUP % 2
                pe.wait_ge(s_qk_out, count(body, first + GROUP, qk_tiles // GROUP))
                for t in range(tiles):
                    for j in range(quads):
                        if t == 0:
                            wait(pe, s_biased, count(body, graph - 1, quads, j + 1))
                        of = slice(j * head, (j + 1) * head)
                        last = nc.tensor.matmul(ps_scores[j][:, t * nodes:(t + 1) * nodes],
                                                qk_t[of, pair, t, graph % GROUP, :],
                                                qk_t[of, pair, tiles + t, graph % GROUP, :],
                                                start=True, stop=True)
                        if t == tiles - 1:
                            last.then_inc(s_scores, 1)

            def transpose_attn(body, graph, t):
                n = (graph % SLOTS) * tiles + t
                pe.wait_ge(s_attn, count(body, graph, tiles, t + 1))
                wait(pe, s_attn_t_out, count(body, graph, tiles, t - 1))
                for j in range(quads):
                    last = nc.tensor.transpose(ps_attn[n % 2][:, j * nodes:(j + 1) * nodes],
                                               attn[:, graph % 2, t * quads + j, :], identity[:])
                last.then_inc(s_attn_t, 1)

            def attend(body, s, graph):
                ps = bank(body, s, "av")
                pe.wait_ge(s_attn_t_out, count(body, graph + 1, tiles))
                pe.wait_ge(s_v_out, count(body, graph, 1, 1))
                for t in range(tiles):
                    for j in range(quads):
                        c = (t * quads + j) * head
                        last = nc.tensor.matmul(ps[j * head:(j + 1) * head, t * nodes:(t + 1) * nodes],
                                                v_rows[:, graph % SLOTS, c:c + head],
                                                attn_t[:, graph % 2, t * quads + j, :],
                                                start=True, stop=True)
                last.then_inc(s_av, 1)

            def project_out(body, s, graph):
                ps = bank(body, s, "o")
                pe.wait_ge(s_o_lo, count(body, graph, 1, 1))
                wait_for_weight(body, graph, w_names.index("o"))
                split_product(ps[:, 0:width],
                              lambda a, t: (o_hi, o_lo)[a][:, graph % 2, t, :],
                              lambda b, t: (w_hi, w_lo)[b]["o"][:, t, :]).then_inc(s_o, 1)

            def step(body, s):
                now = group_of(s)
                ahead = there(body, now + GROUP)
                k = s % GROUP
                if k == 0 and ahead:
                    transpose_h(body, s, now + GROUP, 0)
                if there(body, s):
                    make_scores(body, s)
                if k == 0 and ahead:
                    transpose_h(body, s, now + GROUP, 1)
                if there(body, s - 3):
                    project_out(body, s, s - 3)
                if ahead:
                    project_qk(body, s, now + GROUP, 3 * k)
                if there(body, s - 2):
                    transpose_attn(body, s - 2, 0)
                    transpose_attn(body, s - 2, 1)
                if ahead:
                    project_qk(body, s, now + GROUP, 3 * k + 1)
                if there(body, s - 2):
                    transpose_attn(body, s - 2, 2)
                if ahead:
                    project_qk(body, s, now + GROUP, 3 * k + 2)
                if there(body, s - 2):
                    attend(body, s, s - 2)
                if ahead:
                    project_v(body, s, now + GROUP, k)

            pe.wait_ge(s_constants, 4)
            run(pe, step, GROUP)

        @block.scalar
        def _(act):
            def round_weight(n):
                act.wait_ge(s_weights[n], DMA)
                nc.scalar.activation(w_hi[n][:], w_full[n][:], ACT.Copy).then_inc(s_w_hi, 1)

            def round_h(body, first, g):
                wait(act, s_qk, count(body, first, qk_tiles // GROUP))
                wait(act, s_v, count(body, first))
                act.wait_ge(s_h_t, count(body, first + g, 1, 1))
                nc.scalar.activation(h_hi[:, :, g, :],
                                     ps_turn[turn(first - GROUP, f"h_t{g}") % 2][:, 0:width].rearrange(
                                         "p (t n) -> p t n", t=tiles), ACT.Relu).then_inc(s_h_hi, 1)

            def copy_qk(body, first, tile):
                pair = first // GROUP % 2
                act.wait_ge(s_qk, count(body, first, qk_tiles // GROUP, tile + 1))
                wait(act, s_scores, count(body, first - GROUP, quads))
                nc.scalar.activation(qk_t[:, pair, tile, :, :],
                                     ps_turn[turn(first - GROUP + tile // 3, f"qk{tile}") % 2][
                                         :, 0:GROUP * nodes].rearrange("p (g n) -> p g n", g=GROUP),
                                     ACT.Copy).then_inc(s_qk_out, 1)

            def copy_attn_t(body, graph, t):
                n = (graph % SLOTS) * tiles + t
                act.wait_ge(s_attn_t, count(body, graph, tiles, t + 1))
                wait(act, s_av, count(body, graph - 1))
                nc.scalar.activation(attn_t[:, graph % 2, t * quads:(t + 1) * quads, :],
                                     ps_attn[n % 2][:].rearrange("p (j n) -> p j n", j=quads),
                                     ACT.Copy).then_inc(s_attn_t_out, 1)

            def exponentials(body, graph, part):
                b = graph % 2
                if part == 0:
                    act.wait_ge(s_max, count(body, graph, 1, 1))
                    wait(act, s_attn, count(body, graph - 1, tiles))
                for h in (2 * part, 2 * part + 1):
                    last = nc.scalar.activation(probs[:, b, h, :], scores[:, b, h // quads, h % quads, :],
                                                ACT.Exp, bias=minus_max[:, b, h:h + 1],
                                                accum_out=sums[:, b, h:h + 1])
                if h == HEADS - 1:
                    last.then_inc(s_exp, 1)

            def round_o(body, graph):
                act.wait_ge(s_av, count(body, graph, 1, 1))
                wait(act, s_o, count(body, graph - 1))
                nc.scalar.activation(o_hi[:, graph % 2, :, :],
                                     ps_turn[turn(graph + 2, "av") % 2][:, 0:width].rearrange(
                                         "p (t n) -> p t n", t=tiles), ACT.Copy).then_inc(s_o_hi, 1)

            def step(body, s):
                now = group_of(s)
                ahead = there(body, now + GROUP)
                k = s % GROUP
                start = isinstance(body, int) and SLOTS * body + s == -GROUP
                for g in range(GROUP):
                    if start:
                        round_weight("qk"[g])
                    if k == 0 and ahead:
                        round_h(body, now + GROUP, g)
                    if there(body, s - 1):
                        for part in range(3 * g, 3 * g + 3):
                            exponentials(body, s - 1, part)
                if start:
                    round_weight("v")
                if ahead:
                    copy_qk(body, now + GROUP, 3 * k)
                if there(body, s - 2):
                    copy_attn_t(body, s - 2, 0)
                    copy_attn_t(body, s - 2, 1)
                if ahead:
                    copy_qk(body, now + GROUP, 3 * k + 1)
                if there(body, s - 2):
                    copy_attn_t(body, s - 2, 2)
                if ahead:
                    copy_qk(body, now + GROUP, 3 * k + 2)
                if there(body, s - 2):
                    round_o(body, s - 2)
                if start:
                    round_weight("o")

            run(act, step, GROUP)

        @block.vector
        def _(dve):
            def rest_of_weight(n):
                dve.wait_ge(s_w_hi, w_names.index(n) + 1)
                nc.vector.tensor_tensor(w_lo[n][:], w_full[n][:], w_hi[n][:].bitcast(F32),
                                        ALU.subtract).then_inc(s_w_lo, 1)

            def statistics(body, graph):
                slot = graph % SLOTS
                dve.wait_ge(s_x[slot], DMA * (body + (graph // SLOTS + 1)))
                nc.vector.bn_stats(bn_parts[:, slot, :], x_in[:, slot, :]).then_inc(s_parts, 1)

            def wait_for_mean(body, graph):
                dve.wait_ge(s_parts, count(body, graph, 1, 1))
                wait(dve, s_h, count(body, graph - SLOTS, 1, 1))

            def mean(body, graph):
                slot = graph % SLOTS
                nc.vector.bn_aggr(mean_var[:, slot, :], bn_parts[:, slot, :]).then_inc(s_stats, 1)

            def rest_of_h(body, first, g):
                dve.wait_ge(s_h_hi, count(body, first + g, 1, 1))
                nc.vector.scalar_tensor_tensor(
                    out=h_lo[:, :, g, :],
                    in0=ps_turn[turn(first - GROUP, f"h_t{g}") % 2][:, 0:width].rearrange(
                        "p (t n) -> p t n", t=tiles),
                    scalar=0.0, in1=h_hi[:, :, g, :].bitcast(F32),
                    op0=ALU.max, op1=ALU.subtract).then_inc(s_h_lo, 1)

            def bias_v(body, first, g):
                dve.wait_ge(s_v, count(body, first + g, 1, 1))
                wait(dve, s_av, count(body, first + g - SLOTS, 1, 1))
                nc.vector.tensor_tensor(v_rows[:, (first + g) % SLOTS, :],
                                        ps_turn[turn(first - GROUP + g, f"v{g}") % 2][:, 0:width],
                                        bv_rows[:], ALU.add).then_inc(s_v_out, 1)

            def bias_scores(body, graph, banks):
                slot = graph % SLOTS
                dve.wait_ge(s_adj[slot], DMA * (body + (graph // SLOTS + 1)))
                wait(dve, s_exp, count(body, graph - 1))
                for j in banks:
                    dve.wait_ge(s_scores, count(body, graph, quads, j + 1))
                    nc.vector.scalar_tensor_tensor(
                        out=scores[:, graph % 2, :, j, :],
                        in0=ps_scores[j][:, 0:tiles * nodes].rearrange("p (t m) -> p t m", t=tiles),
                        scalar=scale,
                        in1=adj_in[:, slot:slot + 1, :].to_broadcast([128, tiles, nodes]),
                        op0=ALU.mult, op1=ALU.add).then_inc(s_biased, 1)

            def maxima(body, graph):
                dve.wait_ge(s_biased, count(body, graph + 1, quads))
                of = scores[:, graph % 2, :, :, :].rearrange("p t j m -> p (t j) m")
                nc.vector.tensor_reduce(minus_max[:, graph % 2, :], of, AX_X, ALU.max,
                                        negate=True).then_inc(s_max, 1)

            def zero_rows(body, graph):
                of = scores[:, graph % 2, :, :, :].rearrange("p t j m -> p (t j) m")
                nc.vector.tensor_reduce(max_abs[:, graph % 2, :], of, AX_X, ALU.max,
                                        apply_absolute_value=True).then_inc(s_abs, 1)

            def factors(body, graph):
                b = graph % 2
                dve.wait_ge(s_exp, count(body, graph, 1, 1))
                nc.vector.reciprocal(inverse[:, b, :], sums[:, b, :]).then_inc(s_inverse, 1)
                dve.wait_ge(s_inverse, count(body, graph, 1, 1))
                dve.wait_ge(s_abs, count(body, graph, 1, 1))
                wait(dve, s_attn, count(body, graph - 1, tiles))
                nc.vector.scalar_tensor_tensor(out=factor[:, b, :], in0=max_abs[:, b, :], scalar=0.0,
                                               in1=inverse[:, b, :], op0=ALU.is_gt,
                                               op1=ALU.mult).then_inc(s_factor, 1)

            def rest_of_o(body, graph):
                dve.wait_ge(s_o_hi, count(body, graph, 1, 1))
                nc.vector.tensor_tensor(
                    o_lo[:, graph % 2, :, :],
                    ps_turn[turn(graph + 2, "av") % 2][:, 0:width].rearrange("p (t n) -> p t n", t=tiles),
                    o_hi[:, graph % 2, :, :].bitcast(F32), ALU.subtract).then_inc(s_o_lo, 1)

            def make_out(body, graph):
                slot = graph % SLOTS
                dve.wait_ge(s_o, count(body, graph, 1, 1))
                dve.wait_ge(s_x_bo, count(body, graph, 1, 1))
                wait(dve, s_stored[slot], DMA * (body + graph // SLOTS))
                nc.vector.tensor_tensor(out_rows[:, slot, :],
                                        ps_turn[turn(graph + 3, "o") % 2][:, 0:width],
                                        x_bo[:, slot, :], ALU.add).then_inc(s_out, 1)

            def step(body, s):
                now = group_of(s)
                ahead = there(body, now + GROUP)
                k = s % GROUP
                start = isinstance(body, int) and SLOTS * body + s == -GROUP
                if start:
                    rest_of_weight("q")
                if k == 0 and ahead:
                    rest_of_h(body, now + GROUP, 0)
                if there(body, s - 1):
                    zero_rows(body, s - 1)
                if k == 0 and ahead:
                    rest_of_h(body, now + GROUP, 1)
                if start:
                    rest_of_weight("k")
                    rest_of_weight("v")
                    dve.wait_ge(s_bv, DMA)
                if there(body, s):
                    bias_scores(body, s, range(quads // 2))
                if there(body, s - 3):
                    make_out(body, s - 3)
                if there(body, s):
                    bias_scores(body, s, range(quads // 2, quads))
                if there(body, s - 1):
                    factors(body, s - 1)
                if there(body, s):
                    maxima(body, s)
                if there(body, s + SLOTS):
                    statistics(body, s + SLOTS)
                    wait_for_mean(body, s + SLOTS)
                if there(body, s - 2):
                    rest_of_o(body, s - 2)
                if there(body, s + SLOTS):
                    mean(body, s + SLOTS)
                if ahead:
                    bias_v(body, now + GROUP, k)
                if isinstance(body, int) and SLOTS * body + s == 1:
                    rest_of_weight("o")

            run(dve, step, SLOTS, peeled=2)


_INS = ["x", "adj", "L0_gnn_Wq", "L0_gnn_Wk", "L0_gnn_Wv", "L0_gnn_Wo", "L0_gnn_bv", "L0_gnn_bo"]


def kernel(**inputs):
    import numpy as np
    import concourse.bacc as bacc
    from concourse.bass_utils import run_bass_kernel_spmd

    nc = bacc.Bacc("TRN2", target_bir_lowering=False, num_devices=1)
    arrays, args = {}, []
    for name in _INS:
        a = np.asarray(inputs[name])
        if "_W" in name:
            a = a.T
        a = np.ascontiguousarray(a)
        arrays[f"in_{name}"] = a
        args.append(nc.dram_tensor(f"in_{name}", a.shape, mybir.dt.from_np(a.dtype), kind="ExternalInput").ap())
    shape = inputs["x"].shape
    args.append(nc.dram_tensor("out_rows_dram", shape, F32, kind="ExternalOutput").ap())
    attention_layer(nc, *args)
    r = run_bass_kernel_spmd(nc, [arrays], core_ids=[0])
    return r.results[0]["out_rows_dram"]
```
